# Optimizing a Trainium2 kernel written in Bass

```python
import numpy as np
import jax
import jax.numpy as jnp

def _softmax(x, axis=-1):
    return jax.nn.softmax(x, axis=axis)

def _gelu(x):
    return jax.nn.gelu(x, approximate=True)

def _silu(x):
    return jax.nn.silu(x)

def _sigmoid(x):
    return jax.nn.sigmoid(x)

def _layernorm(x, axis=-1, eps=1e-05):
    m = jnp.mean(x, axis=axis, keepdims=True)
    v = jnp.var(x, axis=axis, keepdims=True)
    return (x - m) / jnp.sqrt(v + eps)

def _scatter_add(tgt, idx, src, axis=0):
    return tgt.at[idx].add(src)

def _segment_sum(src, seg, n):
    return jax.ops.segment_sum(src, seg, n)
kernel_name = 'mk_sandwich_d1_jaxref_r4_d12b7d'

def setup_inputs(seed: int=0):
    np.random.seed(seed)
    _w = jnp.asarray

    def _L0_attn_setup():
        import jax, jax.numpy as jnp
        import numpy as np
        import math
        N_HEADS = 16
        DIM = 256
        B, S = (2, 512)

        def _split_heads(x, n_heads):
            b, s, d = x.shape
            dh = d // n_heads
            return x.reshape(b, s, n_heads, dh).transpose(0, 2, 1, 3)
        key = jax.random.key(seed)
        ks = jax.random.split(key, 9)
        std = 0.02
        inp = {'query': jax.random.normal(ks[0], (B, S, DIM), dtype=jnp.float32), 'mask': jnp.ones((B, S), dtype=jnp.int64), 'q_w': jax.random.normal(ks[1], (DIM, DIM), dtype=jnp.float32) * std, 'q_b': jnp.zeros((DIM,), dtype=jnp.float32), 'k_w': jax.random.normal(ks[2], (DIM, DIM), dtype=jnp.float32) * std, 'k_b': jnp.zeros((DIM,), dtype=jnp.float32), 'v_w': jax.random.normal(ks[3], (DIM, DIM), dtype=jnp.float32) * std, 'v_b': jnp.zeros((DIM,), dtype=jnp.float32), 'out_w': jax.random.normal(ks[4], (DIM, DIM), dtype=jnp.float32) * std, 'out_b': jnp.zeros((DIM,), dtype=jnp.float32)}
        return inp
    _L0_attn_in = _L0_attn_setup()

    def _L0_ffn_setup():
        import jax, jax.numpy as jnp
        import numpy as np
        B, L, D = (4, 256, 256)
        E, H, K = (16, 128, 8)
        EPS = 1e-12

        def _l2norm(v, axis=-1):
            n = jnp.sqrt(jnp.sum(v * v, axis=axis, keepdims=True))
            return v / jnp.maximum(n, EPS)
        if __name__ == '__main__':
            out = reference(**setup_inputs())
            print(out.shape)
        key = jax.random.key(seed)
        ks = jax.random.split(key, 8)
        s = lambda fan_in: 1.0 / np.sqrt(fan_in)
        return {'x': jax.random.normal(ks[0], (B, L, D), jnp.float32), 'gate_w': jax.random.normal(ks[1], (E, D), jnp.float32) * s(D), 'w_gate': jax.random.normal(ks[2], (E, D, H), jnp.float32) * s(D), 'w_up': jax.random.normal(ks[3], (E, D, H), jnp.float32) * s(D), 'w_down': jax.random.normal(ks[4], (E, H, D), jnp.float32) * s(H), 'sw_gate': jax.random.normal(ks[5], (D, H), jnp.float32) * s(D), 'sw_up': jax.random.normal(ks[6], (D, H), jnp.float32) * s(D), 'sw_down': jax.random.normal(ks[7], (H, D), jnp.float32) * s(H)}
    _L0_ffn_in = _L0_ffn_setup()
    _d = {'L0_attn_query': _L0_attn_in['query'], 'L0_attn_mask': _L0_attn_in['mask'], 'L0_attn_q_w': _L0_attn_in['q_w'], 'L0_attn_q_b': _L0_attn_in['q_b'], 'L0_attn_k_w': _L0_attn_in['k_w'], 'L0_attn_k_b': _L0_attn_in['k_b'], 'L0_attn_v_w': _L0_attn_in['v_w'], 'L0_attn_v_b': _L0_attn_in['v_b'], 'L0_attn_out_w': _L0_attn_in['out_w'], 'L0_attn_out_b': _L0_attn_in['out_b'], 'L0_ffn_gate_w': _L0_ffn_in['gate_w'], 'L0_ffn_w_gate': _L0_ffn_in['w_gate'], 'L0_ffn_w_up': _L0_ffn_in['w_up'], 'L0_ffn_w_down': _L0_ffn_in['w_down'], 'L0_ffn_sw_gate': _L0_ffn_in['sw_gate'], 'L0_ffn_sw_up': _L0_ffn_in['sw_up'], 'L0_ffn_sw_down': _L0_ffn_in['sw_down']}
    _x0 = _d['L0_attn_query']
    _d['L0_attn_query'] = jax.random.normal(jax.random.fold_in(jax.random.key(seed), 1), (8, 1024, 256), dtype=_x0.dtype)
    del _x0
    return _d

def reference(L0_attn_query, L0_attn_mask, L0_attn_q_w, L0_attn_q_b, L0_attn_k_w, L0_attn_k_b, L0_attn_v_w, L0_attn_v_b, L0_attn_out_w, L0_attn_out_b, L0_ffn_gate_w, L0_ffn_w_gate, L0_ffn_w_up, L0_ffn_w_down, L0_ffn_sw_gate, L0_ffn_sw_up, L0_ffn_sw_down):

    def _L0_attn_ref(query, mask, q_w, q_b, k_w, k_b, v_w, v_b, out_w, out_b):
        import jax, jax.numpy as jnp
        import numpy as np
        import math
        N_HEADS = 16
        DIM = 256
        B, S = (2, 512)

        def _split_heads(x, n_heads):
            b, s, d = x.shape
            dh = d // n_heads
            return x.reshape(b, s, n_heads, dh).transpose(0, 2, 1, 3)
        b, s, d = query.shape
        h = N_HEADS
        dh = d // h
        scale = math.sqrt(dh)
        q = _split_heads(query @ q_w.T + q_b, h) / scale
        k = _split_heads(query @ k_w.T + k_b, h)
        v = _split_heads(query @ v_w.T + v_b, h)
        scores = jnp.einsum('bhqd,bhkd->bhqk', q, k)
        attn = jax.nn.softmax(scores.astype(jnp.float32), axis=-1).astype(query.dtype)
        ctx = jnp.einsum('bhqk,bhkd->bhqd', attn, v)
        ctx = ctx.transpose(0, 2, 1, 3).reshape(b, s, d)
        out = ctx @ out_w.T + out_b
        return out

    def _L0_ffn_ref(x, gate_w, w_gate, w_up, w_down, sw_gate, sw_up, sw_down):
        import jax, jax.numpy as jnp
        import numpy as np
        B, L, D = (4, 256, 256)
        E, H, K = (16, 128, 8)
        EPS = 1e-12

        def _l2norm(v, axis=-1):
            n = jnp.sqrt(jnp.sum(v * v, axis=axis, keepdims=True))
            return v / jnp.maximum(n, EPS)
        if __name__ == '__main__':
            out = reference(**setup_inputs())
            print(out.shape)
        b, l, d = x.shape
        xf = x.reshape(-1, d)
        logits = _l2norm(xf) @ _l2norm(gate_w).T
        scores = jax.nn.sigmoid(logits)
        topk_scores, topk_idx = jax.lax.top_k(scores, K)
        topk_w = topk_scores / jnp.sum(topk_scores, axis=-1, keepdims=True)
        combine = jnp.sum(jax.nn.one_hot(topk_idx, E, dtype=xf.dtype) * topk_w[..., None], axis=1)
        g = jnp.einsum('nd,edh->neh', xf, w_gate)
        u = jnp.einsum('nd,edh->neh', xf, w_up)
        y = jnp.einsum('neh,ehd->ned', jax.nn.silu(g) * u, w_down)
        routed = jnp.einsum('ned,ne->nd', y, combine)
        shared = jax.nn.silu(xf @ sw_gate) * (xf @ sw_up) @ sw_down
        return (routed + shared).reshape(b, l, d)
    x = L0_attn_query
    x = x + _layernorm(_L0_attn_ref(_layernorm(x, axis=-1), L0_attn_mask, L0_attn_q_w, L0_attn_q_b, L0_attn_k_w, L0_attn_k_b, L0_attn_v_w, L0_attn_v_b, L0_attn_out_w, L0_attn_out_b), axis=-1)
    x = x + _layernorm(_L0_ffn_ref(_layernorm(x, axis=-1), L0_ffn_gate_w, L0_ffn_w_gate, L0_ffn_w_up, L0_ffn_w_down, L0_ffn_sw_gate, L0_ffn_sw_up, L0_ffn_sw_down), axis=-1)
    return x

_drawn_inputs = setup_inputs


def setup_inputs(seed=0):
    import zlib

    import numpy as np

    out = dict(_drawn_inputs(seed))
    spreads = {'L0_attn_q_b': (0.0, 0.8),
     'L0_attn_k_b': (0.0, 0.8),
     'L0_attn_v_b': (0.0, 0.1),
     'L0_attn_out_b': (0.0, 0.1)}
    factors = {'L0_attn_q_w': 4.492, 'L0_attn_k_w': 4.438}
    for name, (base, spread) in spreads.items():
        noise = np.random.default_rng([zlib.crc32(name.encode()), seed]).standard_normal(out[name].shape)
        drawn = base * np.exp(spread * noise) if base else spread * noise
        out[name] = jnp.asarray(drawn.astype(out[name].dtype))
    for name, factor in factors.items():
        out[name] = (out[name] * factor).astype(out[name].dtype)
    return out
```

```python
import concourse.bass as bass
from concourse import mybir
from contextlib import ExitStack

BATCHES, SEQ, D = 8, 1024, 256
HEADS = 16
DH = D // HEADS
CH = 128
CHUNKS = SEQ // CH
HALF = SEQ // 2
HC = HALF // CH
KD = D // 128
QUADS = HEADS // 4
STEPS = 2 * QUADS
UNITS = STEPS * CHUNKS
VW = DH + 1
EXPERTS, HID, TOPK = 16, 128, 8
ALL_E = EXPERTS + 1
TOKENS = BATCHES * SEQ
GROUP = 512
GROUPS = TOKENS // GROUP
EPS = 1e-5
RSQRT_SEED = 0x5F3759DF

F32 = mybir.dt.float32
F32R = mybir.dt.float32r
I32 = mybir.dt.int32
ALU = mybir.AluOpType
ACT = mybir.ActivationFunctionType
AX_X = mybir.AxisListType.X

PARTS = [(0, 0), (1, 0), (0, 1)]

JOBS = {
    0: ("CT", -1, 0), 2: ("OT", -1, 7), 3: ("CT", -1, 1), 5: ("OP", -1, 0), 7: ("OP", -1, 1),
    11: ("CT", -1, 2), 12: ("CT", -1, 3), 45: ("OP", -1, 2), 46: ("OP", -1, 3),
    23: ("XT", 1, 0), 24: ("XT", 1, 1), 27: ("XT", 1, 2), 28: ("XT", 1, 3),
    29: ("QK", 1, 0), 30: ("QK", 1, 1), 31: ("QK", 1, 2), 32: ("QK", 1, 3),
    35: ("QK", 1, 4), 36: ("QK", 1, 5), 37: ("QK", 1, 6), 38: ("QK", 1, 7),
    39: ("V", 1, 0), 40: ("V", 1, 1), 43: ("V", 1, 2), 44: ("V", 1, 3),
}
for _s in range(STEPS):
    JOBS[8 * _s + 1] = ("SH", 0, _s + 1)
    if _s:
        JOBS[8 * _s + 2] = ("OT", 0, _s - 1)
X_STATS = {2: 0, 5: 1, 7: 2, 9: 3, 10: 4, 14: 5, 15: 6, 16: 7}
A_STATS = {29: 0, 30: 1, 47: 2, 48: 3}
RSTD = {17: ("x", 0), 18: ("x", 3), 19: ("x", 6), 20: ("x", 9),
        31: ("a0", 0), 32: ("a0", 3), 36: ("a0", 6), 37: ("a0", 9),
        51: ("a1", 0), 52: ("a1", 3), 53: ("a1", 6), 54: ("a1", 9)}
FIRST_JOBS = [("XT", i) for i in range(4)] + [("QK", i) for i in range(8)]
PER_BATCH = {"XT": 4, "QK": 8, "V": 4, "SH": 8, "OT": 8, "CT": 4, "OP": 4}


def wait_apart(engine, semaphore, value, passed):
    engine.wait_ge(semaphore, value)
    engine.sem_inc(passed, 1)


def attention_stage(nc, x, x1, wq, wk, wv, wo, biases, ob, ident_dram):
    xv = x.rearrange("(n p) d -> p n d", p=CH)
    x1v = x1.rearrange("(n p) d -> p n d", p=CH)
    ctx = ExitStack()
    with ctx:
        def sb(name, shape, dt=F32):
            return ctx.enter_context(nc.sbuf_tensor(name, shape, dt))

        def pb(name, shape):
            return ctx.enter_context(nc.psum_tensor(name, shape, F32))

        def sem(name):
            return ctx.enter_context(nc.semaphore(name))

        ident = sb("ident", [128, 128])
        w_parts = {n: [sb(f"w{n}_hi", [128, KD, D], F32R), sb(f"w{n}_lo", [128, KD, D], F32R)] for n in "qkvo"}
        bias_raw = sb("bias_raw", [128, 3, KD])
        bias = sb("bias", [128, 3, KD])
        out_bias = sb("out_bias", [128, 2, D])
        x_in = sb("x_in", [128, CHUNKS, D])
        xT = [sb("xT_hi", [128, KD, SEQ], F32R), sb("xT_lo", [128, KD, SEQ], F32R)]
        qk_parts = sb("qk_parts", [128, KD, 4, SEQ], F32R)
        compact = {n: [qk_parts[:, :, 2 * i + w, :] for w in range(2)] for i, n in enumerate("qk")}
        qk_stack = [sb(f"qk_stack{q}", [128, 2, 2, SEQ], F32R) for q in range(QUADS)]
        q_stack = [[qk_stack[q][:, p, 0, :] for p in range(2)] for q in range(QUADS)]
        k_stack = [[qk_stack[q][:, p, 1, :] for p in range(2)] for q in range(QUADS)]
        v_stage = sb("v_stage", [128, CHUNKS, HEADS, VW])
        v_quad = [sb(f"v_quad{q}", [128, CHUNKS, 4 * VW + 16]) for q in range(QUADS)]
        probs = [sb(f"probs{i}", [128, 4, HALF]) for i in range(2)]
        score_max = [sb(f"score_max{f}", [128, 4 * HC, 2]) for f in range(2)]
        row_max = sb("row_max", [128, 4 * HC])
        shift_row = [sb(f"shift_row{f}", [4 * HC, CH], F32R) for f in range(2)]
        o_sb = sb("o_sb", [128, HALF])
        recip = sb("recip", [128, HC, 4, 1])
        ctx_tok = [sb(f"ctx_tok{f}", [128, HC, D]) for f in range(2)]
        cT = [sb("cT_hi", [128, KD, HALF], F32R), sb("cT_lo", [128, KD, HALF], F32R)]
        attn_out = sb("attn_out", [128, HC, D])
        x_res = sb("x_res", [128, HC, D])
        stats = sb("stats", [128, CHUNKS, 6])
        stats_a = sb("stats_a", [128, HC, 6])
        scaled = sb("scaled", [128, KD, D])
        mv_x = sb("mv_x", [128, CHUNKS, 2])
        mv_a = sb("mv_a", [128, HC, 2])
        rstd_x = sb("rstd_x", [128, CHUNKS])
        rstd_a = sb("rstd_a", [128, HC])
        newton = sb("newton", [128, CHUNKS])
        newton_a = sb("newton_a", [128, HC])
        var_x = sb("var_x", [128, CHUNKS])
        var_a = sb("var_a", [128, HC])
        w_raw = {n: probs[0][:, i, :].rearrange("p (k d) -> p k d", k=KD) for i, n in enumerate("qkvo")}

        st_bank = [pb(f"st_bank{p}", [128, 2, HALF]) for p in range(2)]
        sm_bank = [pb(f"sm_bank{e}", [128, HALF]) for e in range(2)]
        o_bank = pb("o_bank", [128, HALF])
        job_bank = pb("job_bank", [128, 512])
        first_bank = [job_bank, o_bank]

        passed = {e: sem(f"passed_{e}") for e in ("dve", "pool", "sp")}
        const_loaded = sem("const_loaded")
        ones_set = sem("ones_set")
        stacks_set = sem("stacks_set")
        bias_set = sem("bias_set")
        weights_split = sem("weights_split")
        x_loaded = sem("x_loaded")
        x_normed = sem("x_normed")
        mean_x_ready = sem("mean_x_ready")
        ln_x_chain = sem("ln_x_chain")
        ln_a_chain = sem("ln_a_chain")
        mean_a_ready = sem("mean_a_ready")
        res_loaded = sem("res_loaded")
        x1_ready = sem("x1_ready")
        pool_chain = sem("pool_chain")
        x1_stored = sem("x1_stored")
        stack_loaded = [sem(f"stack_loaded{q}") for q in range(QUADS)]
        v_copied = sem("v_copied")
        st_ready = sem("st_ready")
        exp_done = sem("exp_done")
        pv_done = sem("pv_done")
        smax_ready = sem("smax_ready")
        smax_read = sem("smax_read")
        row_max_ready = sem("row_max_ready")
        recip_ready = sem("recip_ready")
        shift_loaded = sem("shift_loaded")
        o_stored = sem("o_stored")
        job_ready = {k: sem(f"{k}_ready") for k in PER_BATCH}
        job_read = {k: sem(f"{k}_read") for k in PER_BATCH}
        job_hi = {k: sem(f"{k}_hi") for k in ("XT", "QK", "CT")}

        def nth(kind, B, i):
            return B * PER_BATCH[kind] + (i + 1)

        STACK_INC = 16 * (4 * 3 + 2)

        block = ctx.enter_context(nc.Block())

        @block.sync
        def _(sp):
            sp.dma_start(x_in[:, :, :], xv[:, 0:CHUNKS, :]).then_inc(x_loaded, 16)
            sp.dma_start(ident[:, :], ident_dram).then_inc(const_loaded, 16)
            for n, w in (("q", wq), ("k", wk), ("v", wv), ("o", wo)):
                sp.dma_start(w_raw[n], w.rearrange("(k p) d -> p k d", p=128)).then_inc(const_loaded, 16)
            sp.dma_start(bias_raw[:, :, :], biases).then_inc(const_loaded, 16)
            for i in range(2):
                sp.dma_start(out_bias[:, i, :], ob.partition_broadcast(128)).then_inc(const_loaded, 16)

            def load_x(B):
                wait_apart(sp, job_ready["XT"], nth("XT", B - 1, 3), passed["sp"])
                sp.dma_start(x_in[:, :, :], xv[:, bass.ds(B * CHUNKS, CHUNKS), :]).then_inc(x_loaded, 16)

            def load_stack(B, q, first):
                m = q // 2
                sp.wait_ge(job_read["QK"], nth("QK", B, 4 * m + 3))
                if not first:
                    sp.wait_ge(st_ready, 2 * (UNITS * (B - 1) + 16 * (q + 1)))
                for j in range(4):
                    h, p, base = 4 * q + j, j // 2, 64 * (j % 2)
                    src = slice(DH * (h % 8), DH * (h % 8) + DH)
                    for rows, pair in ((0, slice(0, 4, 2)), (16, slice(1, 3)), (48, slice(0, 4, 3))):
                        sp.dma_start(qk_stack[q][base + rows:base + rows + DH, p, :, :].bitcast(F32),
                                     qk_parts[src, m, pair, :].bitcast(F32)).then_inc(stack_loaded[q], 16)
                for base in (0, 64):
                    sp.dma_start(qk_stack[q][base + 32:base + 33, :, 0, :].bitcast(F32),
                                 qk_stack[q][base + 33:base + 34, :, 0, :].bitcast(F32)).then_inc(stack_loaded[q], 16)

            def load_shift(B, s):
                q, f = (s // 2) % QUADS, s % 2
                sp.wait_ge(job_read["SH"], nth("SH", B, s))
                for j in range(4):
                    row = 64 * (j % 2) + 32
                    sp.dma_start(q_stack[q][j // 2][row:row + 1, f * HALF:(f + 1) * HALF].bitcast(F32),
                                 shift_row[f][HC * j:HC * (j + 1), :].bitcast(F32)).then_inc(shift_loaded, 16)

            def load_residual(B, f):
                wait_apart(sp, x1_stored, 16 * (2 * B + f + 1), passed["sp"])
                sp.dma_start(x_res[:, :, :], xv[:, bass.ds(B * CHUNKS + f * HC, HC), :]).then_inc(res_loaded, 16)

            def store_x1(B, f):
                wait_apart(sp, x1_ready, 2 * B + f + 2, passed["sp"])
                sp.dma_start(x1v[:, bass.ds(B * CHUNKS + f * HC, HC), :], x_res[:, :, :]).then_inc(x1_stored, 16)

            sp.sem_inc(x1_stored, 16)
            for q in range(3):
                sp.wait_ge(stacks_set, 5 * (q + 1))
                load_stack(0, q, True)
            load_x(1)
            load_shift(0, 0)

            def batch(b, first, last, next_last):
                if not first:
                    load_residual(b - 1, 0)
                load_shift(b, 1)
                if first:
                    sp.wait_ge(stacks_set, 5 * QUADS)
                load_stack(b, 3, first)
                load_shift(b, 2)
                load_shift(b, 3)
                load_shift(b, 4)
                if not (last or next_last):
                    load_x(b + 2)
                load_shift(b, 5)
                if not last:
                    load_stack(b + 1, 0, False)
                load_shift(b, 6)
                if not first:
                    store_x1(b - 1, 0)
                    load_residual(b - 1, 1)
                if not last:
                    load_stack(b + 1, 1, False)
                load_shift(b, 7)
                if not last:
                    load_stack(b + 1, 2, False)
                    load_shift(b, 8)
                if not first:
                    store_x1(b - 1, 1)

            batch(0, True, False, False)
            with sp.Fori(1, BATCHES - 2) as b:
                batch(b, False, False, False)
            batch(BATCHES - 2, False, False, True)
            batch(BATCHES - 1, False, True, False)
            load_residual(BATCHES - 1, 0)
            store_x1(BATCHES - 1, 0)
            load_residual(BATCHES - 1, 1)
            store_x1(BATCHES - 1, 1)
            sp.wait_ge(x1_stored, 16 * (2 * BATCHES + 1))

        @block.tensor
        def _(pe):
            mm = nc.tensor.matmul
            before = []

            def st(U, s, kc, p, new_step):
                q, f = s // 2, s % 2
                if new_step is not None:
                    pe.wait_ge(shift_loaded, 64 * (new_step + 1))
                if not (isinstance(U, int) and U == 0):
                    pe.wait_ge(exp_done, 2 * (U - 1) + p + 1)
                for e in range(2):
                    rows = slice(64 * e, 64 * e + 64)
                    last = mm(st_bank[p][:, e, :], k_stack[q][p][rows, kc * CH:(kc + 1) * CH],
                              q_stack[q][p][rows, f * HALF:(f + 1) * HALF], start=True, stop=True)
                last.then_inc(st_ready, 1)

            def smax(S, s, kc, half, e):
                q, f = s // 2, s % 2
                p, c = kc // HC, kc % HC
                tok = f * HALF + c * CH
                n = 32 * S + 4 * kc + 2 * half + e
                if not (isinstance(n, int) and n < 2):
                    pe.wait_ge(smax_read, n - 1)
                rows = slice(64 * e, 64 * e + 64)
                mm(sm_bank[e][:, :], q_stack[q][p][rows, tok:tok + CH],
                   k_stack[q][p][rows, half * HALF:(half + 1) * HALF], start=True, stop=True).then_inc(smax_ready, 1)

            def pv(U, S, s, kc):
                q = s // 2
                if kc == 0 and not (isinstance(S, int) and S == 0):
                    pe.wait_ge(o_stored, S)
                pe.wait_ge(exp_done, 2 * U + 2)
                for j in range(4):
                    last = mm(o_bank[32 * j:32 * j + 32, :], v_quad[q][:, kc, VW * j:VW * j + 32],
                              probs[0 if kc % 2 == 0 else 1][:, j, :], start=(kc == 0), stop=(kc == CHUNKS - 1))
                last.then_inc(pv_done, 1)

            def nothing():
                pass

            def job(kind, B, i, between=nothing, job_bank=job_bank, banks=1):
                halfway = [between]
                if len(before) == banks:
                    k0, B0, i0 = before.pop(0)
                    pe.wait_ge(job_read[k0], nth(k0, B0, i0))
                before.append((kind, B, i))
                if kind == "XT":
                    half, k = i // 2, i % 2
                    pe.wait_ge(x_normed, B * CHUNKS + HC * (half + 1))
                    for c in range(HC):
                        last = nc.tensor.transpose(job_bank[:, c * CH:(c + 1) * CH],
                                                   x_in[:, half * HC + c, k * 128:(k + 1) * 128], ident[:, :])
                elif kind == "QK":
                    m, half, n = i // 4, i // 2 % 2, "qk"[i % 2]
                    pe.wait_ge(job_read["XT"], nth("XT", B, 2 * half + 1))
                    steps = [(k, a, w) for k in range(KD) for a, w in PARTS]
                    for t, (k, a, w) in enumerate(steps):
                        if t == 3:
                            halfway.pop()()
                        last = mm(job_bank[:, :], w_parts[n][w][:, k, m * 128:(m + 1) * 128],
                                  xT[a][:, k, half * HALF:(half + 1) * HALF], start=(t == 0), stop=(t == len(steps) - 1))
                elif kind == "V":
                    pe.wait_ge(job_read["XT"], nth("XT", B, 3))
                    steps = [(k, a, w) for k in range(KD) for a, w in PARTS]
                    for c in (2 * i, 2 * i + 1):
                        if c % 2:
                            halfway.pop()()
                        for t, (k, a, w) in enumerate(steps):
                            last = mm(job_bank[:, (c % 2) * D:(c % 2 + 1) * D], xT[a][:, k, c * CH:(c + 1) * CH],
                                      w_parts["v"][w][:, k, :], start=(t == 0), stop=(t == len(steps) - 1))
                elif kind == "SH":
                    pe.wait_ge(row_max_ready, nth("SH", B, i))
                    last = nc.tensor.transpose(job_bank[0:4 * HC, 0:CH], row_max[:, :], ident[:, :])
                elif kind == "OT":
                    pe.wait_ge(o_stored, nth("OT", B, i))
                    for c in range(HC):
                        last = nc.tensor.transpose(job_bank[:, c * CH:(c + 1) * CH], o_sb[:, c * CH:(c + 1) * CH], ident[:, :])
                elif kind == "CT":
                    f, k = i // 2, i % 2
                    pe.wait_ge(job_read["OT"], nth("OT", B, 6 + f))
                    for c in range(HC):
                        last = nc.tensor.transpose(job_bank[:, c * CH:(c + 1) * CH],
                                                   ctx_tok[f][:, c, k * 128:(k + 1) * 128], ident[:, :])
                else:
                    f, h = i // 2, i % 2
                    pe.wait_ge(job_read["CT"], nth("CT", B, 2 * f + 1))
                    steps = [(k, a, w) for k in range(KD) for a, w in PARTS]
                    for c in (2 * h, 2 * h + 1):
                        if c % 2:
                            halfway.pop()()
                        for t, (k, a, w) in enumerate(steps):
                            last = mm(job_bank[:, (c % 2) * D:(c % 2 + 1) * D], cT[a][:, k, c * CH:(c + 1) * CH],
                                      w_parts["o"][w][:, k, :], start=(t == 0), stop=(t == len(steps) - 1))
                last.then_inc(job_ready[kind], 1)
                if halfway:
                    between()

            pe.wait_ge(const_loaded, 16 * 8)
            for n, (kind, i) in enumerate(FIRST_JOBS):
                if (kind, i) == ("QK", 0):
                    pe.wait_ge(weights_split, 9)
                job(kind, 0, i, job_bank=first_bank[n % 2], banks=2)
            pe.wait_ge(job_read["QK"], nth("QK", 0, 7))
            before.clear()
            pe.wait_ge(stack_loaded[0], STACK_INC)
            for S in range(2):
                for n in range(4 * CHUNKS):
                    smax(S, S, n // 4, n // 2 % 2, n % 2)
                if S == 0:
                    job("SH", 0, 0)
            for i in range(4):
                job("V", 0, i, job_bank=first_bank[(i + 1) % 2], banks=2)
            before.pop(0)
            for p in range(2):
                st(0, 0, 0, p, 0)

            def batch(b, first, last):
                if not first:
                    before.clear()
                    before.append(("OT", b - 1, 6))
                for u in range(UNITS):
                    s, kc = u // CHUNKS, u % CHUNKS
                    U, S = UNITS * b + u, STEPS * b + s
                    maxima = s + 2 < STEPS or not last
                    if kc == 0 and s % 2 == 0:
                        if maxima:
                            B2 = b if s < 6 else b + 1
                            pe.wait_ge(stack_loaded[(s // 2 + 1) % QUADS], STACK_INC * (B2 + 1))
                        pe.wait_ge(v_copied, QUADS * b + s // 2 + 1)
                    def maximum(half, e):
                        if maxima:
                            smax(S + 2, (s + 2) % STEPS, kc, half, e)

                    def scores(p):
                        if u + 1 < UNITS:
                            st(U + 1, (u + 1) // CHUNKS, (u + 1) % CHUNKS, p, S + 1 if kc == CHUNKS - 1 else None)
                        elif not last:
                            st(U + 1, 0, 0, p, S + 1)

                    scores(0)
                    maximum(0, 0)
                    scores(1)
                    maximum(0, 1)
                    pv(U, S, s, kc)
                    maximum(1, 0)
                    kind, off, i = JOBS.get(u, ("", 0, 0))
                    if kind and not (off == -1 and first or off == 1 and last or last and kind == "SH" and i == STEPS):
                        job(kind, b + off, i, lambda: maximum(1, 1))
                    else:
                        maximum(1, 1)

            batch(0, True, False)
            with pe.Fori(1, BATCHES - 1) as b:
                batch(b, False, False)
            batch(BATCHES - 1, False, True)
            job("OT", BATCHES - 1, 7)
            for i in range(2):
                job("CT", BATCHES - 1, i)
            for i in range(2):
                job("OP", BATCHES - 1, i)
            for i in range(2, 4):
                job("CT", BATCHES - 1, i)
            for i in range(2, 4):
                job("OP", BATCHES - 1, i)

        @block.scalar
        def _(act):
            def job(kind, B, i, job_bank=job_bank):
                act.wait_ge(job_ready[kind], nth(kind, B, i))
                if kind == "XT":
                    half, k = i // 2, i % 2
                    if not (isinstance(B, int) and B == 0):
                        act.wait_ge(job_ready["V"], nth("V", B - 1, 3))
                    nc.scalar.activation(xT[0][:, k, half * HALF:(half + 1) * HALF], job_bank[:, :],
                                         ACT.Identity).then_inc(job_hi["XT"], 1)
                elif kind == "QK":
                    m, half, n = i // 4, i // 2 % 2, i % 2
                    if i == 0 and not (isinstance(B, int) and B == 0):
                        act.wait_ge(stack_loaded[3], STACK_INC * B)
                    nc.scalar.activation(compact["qk"[n]][0][:, m, half * HALF:(half + 1) * HALF], job_bank[:, :],
                                         ACT.Identity, bias=bias[:, n, m:m + 1]).then_inc(job_hi["QK"], 1)
                elif kind == "V":
                    if i == 0 and not (isinstance(B, int) and B == 0):
                        act.wait_ge(v_copied, QUADS * B)
                    nc.scalar.activation(v_stage[:, 2 * i:2 * i + 2, :, 0:DH],
                                         job_bank[:, :].rearrange("p (c h d) -> p c h d", c=2, h=HEADS),
                                         ACT.Copy).then_inc(job_read["V"], 1)
                elif kind == "CT":
                    k = i % 2
                    nc.scalar.activation(cT[0][:, k, :], job_bank[:, :], ACT.Identity,
                                         bias=bias[:, 2, k:k + 1]).then_inc(job_hi["CT"], 1)

            act.wait_ge(weights_split, 9)
            act.wait_ge(bias_set, 2)
            act.wait_ge(ones_set, 1)
            for n, (kind, i) in enumerate(FIRST_JOBS):
                job(kind, 0, i, first_bank[n % 2])
            for i in range(4):
                job("V", 0, i, first_bank[(i + 1) % 2])

            def store_o(S):
                act.wait_ge(pv_done, CHUNKS * S)
                if not (isinstance(S, int) and S == 1):
                    act.wait_ge(job_ready["OT"], S - 1)
                nc.scalar.activation(o_sb[:, :], o_bank[:, :], ACT.Copy).then_inc(o_stored, 1)

            def batch(b, first, last):
                for u in range(UNITS):
                    s, kc = u // CHUNKS, u % CHUNKS
                    U, S = UNITS * b + u, STEPS * b + s
                    for p in range(2):
                        act.wait_ge(st_ready, 2 * U + p + 1)
                        if p == 0 and not (first and u < 2):
                            act.wait_ge(pv_done, U - 1)
                        nc.scalar.activation(probs[kc % 2][:, 2 * p:2 * p + 2, :], st_bank[p][:, :, :],
                                             ACT.Exp).then_inc(exp_done, 1)
                    if kc == 0 and not (first and s == 0):
                        store_o(S)
                    if u - 1 in JOBS:
                        kind, off, i = JOBS[u - 1]
                        if kind in ("XT", "QK", "V", "CT") and not (off == -1 and first or off == 1 and last):
                            job(kind, b + off, i)

            batch(0, True, False)
            with act.Fori(1, BATCHES - 1) as b:
                batch(b, False, False)
            batch(BATCHES - 1, False, True)
            store_o(STEPS * BATCHES)
            for i in range(4):
                job("CT", BATCHES - 1, i)

        @block.vector
        def _(dve):
            v = nc.vector

            LN_X = CHUNKS + 12
            LN_A = HC + 12

            def rsqrt_step(n, dst, var, mv, tmp, chain, base):
                if not (isinstance(base, int) and base + n == 0):
                    dve.wait_ge(chain, base + n)
                if n == 0:
                    ins = v.tensor_scalar(var, mv, EPS, None, ALU.add)
                elif n == 1:
                    ins = v.tensor_scalar(dst.bitcast(I32), var.bitcast(I32), 1, None, ALU.logical_shift_right)
                elif n == 2:
                    ins = v.tensor_scalar(dst.bitcast(I32), dst.bitcast(I32), -1, RSQRT_SEED, ALU.mult, ALU.add)
                elif n % 3 == 0:
                    ins = v.scalar_tensor_tensor(tmp, dst, -0.5, dst, ALU.mult, ALU.mult)
                elif n % 3 == 1:
                    ins = v.tensor_tensor(tmp, tmp, var, ALU.mult)
                else:
                    ins = v.scalar_tensor_tensor(dst, tmp, 1.5, dst, ALU.add, ALU.mult)
                ins.then_inc(chain, 1)

            def ln_x_stats(B, c):
                if c == 0:
                    dve.wait_ge(x_loaded, 16 * (B + 1))
                if not (isinstance(B, int) and B == 0):
                    dve.wait_ge(x_normed, CHUNKS * B)
                v.bn_stats(stats[:, c, :], x_in[:, c, :]).then_inc(ln_x_chain, 1)

            def ln_x_aggr(B, c):
                wait_apart(dve, ln_x_chain, LN_X * B + c + 1, passed["dve"])
                v.bn_aggr(mv_x[:, c, :], stats[:, c, :]).then_inc(mean_x_ready, 1)

            def ln_x_rstd(B, n):
                if n == 0:
                    dve.wait_ge(mean_x_ready, CHUNKS * (B + 1))
                rsqrt_step(n, rstd_x[:, :], var_x[:, :], mv_x[:, :, 1], newton[:, :], ln_x_chain, LN_X * B + CHUNKS)

            def ln_a_stats(B, i):
                f, h = i // 2, i % 2
                H = 2 * B + f
                dve.wait_ge(job_read["OP"], nth("OP", B, i))
                for c in (2 * h, 2 * h + 1):
                    v.bn_stats(stats_a[:, c, :], attn_out[:, c, :]).then_inc(ln_a_chain, 1)
                for c in (2 * h, 2 * h + 1):
                    wait_apart(dve, ln_a_chain, LN_A * H + c + 1, passed["dve"])
                    v.bn_aggr(mv_a[:, c, :], stats_a[:, c, :]).then_inc(mean_a_ready, 1)


            def ln_a_rstd(B, f, n):
                H = 2 * B + f
                if n == 0:
                    dve.wait_ge(mean_a_ready, HC * (H + 1))
                rsqrt_step(n, rstd_a[:, :], var_a[:, :], mv_a[:, :, 1], newton_a[:, :], ln_a_chain, LN_A * H + HC)

            def reduce(S, s, kc, half):
                f = s % 2
                p, c = kc // HC, kc % HC
                for e in range(2):
                    n = 32 * S + 4 * kc + 2 * half + e
                    dve.wait_ge(smax_ready, n + 1)
                    v.reduce_max(score_max[f][:, HC * (2 * p + e) + c, half:half + 1], sm_bank[e][:, :],
                                 AX_X).then_inc(smax_read, 1)

            def combine_maxima(S, f):
                dve.wait_ge(smax_read, 32 * (S + 1))
                if not (isinstance(S, int) and S == 0):
                    dve.wait_ge(job_ready["SH"], S)
                v.tensor_tensor(row_max[:, :], score_max[f][:, :, 0], score_max[f][:, :, 1],
                                ALU.max).then_inc(row_max_ready, 1)

            def job(kind, B, i, job_bank=job_bank):
                if kind in ("XT", "QK", "CT"):
                    dve.wait_ge(job_hi[kind], nth(kind, B, i))
                    if kind == "XT":
                        half, k = i // 2, i % 2
                        at = (slice(None), k, slice(half * HALF, (half + 1) * HALF))
                        v.tensor_tensor(xT[1][at], job_bank[:, :], xT[0][at].bitcast(F32),
                                        ALU.subtract).then_inc(job_read[kind], 1)
                    else:
                        if kind == "QK":
                            m, half, n = i // 4, i // 2 % 2, i % 2
                            at = (slice(None), m, slice(half * HALF, (half + 1) * HALF))
                            hi, lo, col = compact["qk"[n]][0][at], compact["qk"[n]][1][at], bias[:, n, m:m + 1]
                        else:
                            k = i % 2
                            hi, lo, col = cT[0][:, k, :], cT[1][:, k, :], bias[:, 2, k:k + 1]
                        v.scalar_tensor_tensor(lo, job_bank[:, :], col, hi.bitcast(F32), ALU.add,
                                               ALU.subtract).then_inc(job_read[kind], 1)
                    return
                if kind == "V":
                    return
                dve.wait_ge(job_ready[kind], nth(kind, B, i))
                if kind == "SH":
                    f = i % 2
                    S = STEPS * B + i
                    if not (isinstance(S, int) and S < 2):
                        dve.wait_ge(shift_loaded, 64 * (S - 1))
                    v.tensor_scalar(shift_row[f][:, :], job_bank[0:4 * HC, 0:CH], -1.0, None,
                                    ALU.mult).then_inc(job_read["SH"], 1)
                elif kind == "OT":
                    q, f = i // 2, i % 2
                    S = STEPS * B + i
                    o4 = job_bank[:, :].rearrange("p (c j w) -> p c j w", c=HC, j=4)
                    v.reciprocal(recip[:, :, :, :], o4[:, :, :, DH:DH + 1]).then_inc(recip_ready, 1)
                    if q == 0 and not (isinstance(B, int) and B == 0):
                        dve.wait_ge(job_ready["CT"], nth("CT", B - 1, 2 * f + 1))
                    dve.wait_ge(recip_ready, S + 1)
                    v.tensor_tensor(ctx_tok[f][:, :, 64 * q:64 * q + 64].rearrange("p c (j w) -> p c j w", j=4),
                                    o4[:, :, :, 0:DH], recip[:, :, :, :].to_broadcast([128, HC, 4, DH]),
                                    ALU.mult).then_inc(job_read["OT"], 1)
                else:
                    f, h = i // 2, i % 2
                    if h == 0:
                        dve.wait_ge(x1_ready, 2 * B + f + 1)
                    v.tensor_tensor(attn_out[:, 2 * h:2 * h + 2, :], job_bank[:, :].rearrange("p (c d) -> p c d", c=2),
                                    out_bias[:, :, :], ALU.add).then_inc(job_read["OP"], 1)

            v.memset(v_stage[:, :, :, :], 1.0).then_inc(ones_set, 1)
            for c in range(CHUNKS):
                ln_x_stats(0, c)
            for c in range(CHUNKS):
                ln_x_aggr(0, c)
            for n in range(12):
                ln_x_rstd(0, n)
            dve.wait_ge(const_loaded, 16 * 8)
            v.tensor_scalar(scaled[:, :, :], w_raw["q"], DH ** -0.5, None, ALU.mult).then_inc(weights_split, 1)
            v.tensor_scalar(bias[:, 0, :], bias_raw[:, 0, :], DH ** -0.5, None, ALU.mult).then_inc(bias_set, 1)
            v.tensor_copy(bias[:, 1:3, :], bias_raw[:, 1:3, :]).then_inc(bias_set, 1)
            dve.wait_ge(bias_set, 2)
            dve.wait_ge(weights_split, 1)
            raw = {"q": scaled[:, :, :], "k": w_raw["k"], "v": w_raw["v"], "o": w_raw["o"]}
            for n in "qkvo":
                v.tensor_copy(w_parts[n][0][:, :, :], raw[n]).then_inc(weights_split, 1)
            for i, n in enumerate("qkvo"):
                dve.wait_ge(weights_split, 2 + i)
                v.tensor_tensor(w_parts[n][1][:, :, :], raw[n], w_parts[n][0][:, :, :].bitcast(F32),
                                ALU.subtract).then_inc(weights_split, 1)

            for n, (kind, i) in enumerate(FIRST_JOBS):
                job(kind, 0, i, first_bank[n % 2])
            for S in range(2):
                for kc in range(CHUNKS):
                    reduce(S, S, kc, 0)
                    reduce(S, S, kc, 1)
                if S == 0:
                    combine_maxima(0, 0)
                    job("SH", 0, 0)

            def batch(b, first, last):
                for u in range(UNITS):
                    s, kc = u // CHUNKS, u % CHUNKS
                    S = STEPS * b + s
                    maxima = s + 2 < STEPS or not last
                    if kc == 0 and not (last and s == STEPS - 1):
                        combine_maxima(S + 1, (s + 1) % 2)
                    if u - 1 in JOBS:
                        kind, off, i = JOBS[u - 1]
                        if not (off == -1 and first or off == 1 and last or last and kind == "SH" and i == STEPS):
                            job(kind, b + off, i)
                    if maxima:
                        reduce(S + 2, (s + 2) % STEPS, kc, 0)
                    if not last and u in X_STATS:
                        ln_x_stats(b + 1, X_STATS[u])
                    if not first and u in A_STATS:
                        ln_a_stats(b - 1, A_STATS[u])
                    if u in RSTD:
                        chain, n0 = RSTD[u]
                        for n in range(n0, n0 + 3):
                            if n == n0 + 2 and maxima:
                                reduce(S + 2, (s + 2) % STEPS, kc, 1)
                            if chain == "x" and not last:
                                ln_x_rstd(b + 1, n)
                            elif chain != "x" and not first:
                                ln_a_rstd(b - 1, int(chain[1]), n)
                    elif maxima:
                        reduce(S + 2, (s + 2) % STEPS, kc, 1)
                    if not last and u in X_STATS:
                        ln_x_aggr(b + 1, X_STATS[u])

            batch(0, True, False)
            with dve.Fori(1, BATCHES - 1) as b:
                batch(b, False, False)
            batch(BATCHES - 1, False, True)
            job("OT", BATCHES - 1, 7)
            for f in range(2):
                job("CT", BATCHES - 1, 2 * f)
                job("CT", BATCHES - 1, 2 * f + 1)
                for i in (2 * f, 2 * f + 1):
                    job("OP", BATCHES - 1, i)
                    ln_a_stats(BATCHES - 1, i)
                for n in range(12):
                    ln_a_rstd(BATCHES - 1, f, n)

        @block.gpsimd
        def _(pool):
            g = nc.gpsimd

            def set_stacks(q):
                g.memset(v_quad[q][:, :, :], 1.0).then_inc(stacks_set, 1)
                for p in range(2):
                    g.memset(q_stack[q][p][:, :].bitcast(F32), 0.0).then_inc(stacks_set, 1)
                    g.memset(k_stack[q][p][:, :].bitcast(F32), 1.0).then_inc(stacks_set, 1)

            def norm_x(B):
                wait_apart(pool, ln_x_chain, (CHUNKS + 12) * (B + 1), passed["pool"])
                for c in range(CHUNKS):
                    g.tensor_scalar(x_in[:, c, :], x_in[:, c, :], mv_x[:, c, 0:1], rstd_x[:, c:c + 1],
                                    ALU.subtract, ALU.mult).then_inc(x_normed, 1)

            def copy_v(B, q, first):
                wait_apart(pool, job_read["V"], nth("V", B, 3), passed["pool"])
                if not first:
                    wait_apart(pool, pv_done, UNITS * (B - 1) + 16 * (q + 1), passed["pool"])
                g.tensor_copy(v_quad[q][:, :, 0:4 * VW].rearrange("p c (h w) -> p c h w", h=4),
                              v_stage[:, :, 4 * q:4 * q + 4, :]).then_inc(v_copied, 1)

            def residual(B, f):
                H = 2 * B + f
                wait_apart(pool, ln_a_chain, (HC + 12) * (H + 1), passed["pool"])
                for c in range(HC):
                    g.tensor_scalar(attn_out[:, c, :], attn_out[:, c, :], mv_a[:, c, 0:1], rstd_a[:, c:c + 1],
                                    ALU.subtract, ALU.mult).then_inc(pool_chain, 1)
                wait_apart(pool, res_loaded, 16 * (H + 1), passed["pool"])
                wait_apart(pool, pool_chain, HC * (H + 1), passed["pool"])
                g.tensor_tensor(x_res[:, :, :], attn_out[:, :, :], x_res[:, :, :], ALU.add).then_inc(x1_ready, 1)

            pool.sem_inc(x1_ready, 1)
            set_stacks(0)
            norm_x(0)
            for q in range(1, QUADS):
                set_stacks(q)
            wait_apart(pool, stacks_set, 5 * QUADS, passed["pool"])
            for q in range(3):
                copy_v(0, q, True)

            def batch(b, first, last):
                copy_v(b, 3, first)
                if not last:
                    norm_x(b + 1)
                if not first:
                    residual(b - 1, 0)
                if not last:
                    for q in range(3):
                        copy_v(b + 1, q, False)
                if not first:
                    residual(b - 1, 1)

            batch(0, True, False)
            with pool.Fori(1, BATCHES - 1) as b:
                batch(b, False, False)
            batch(BATCHES - 1, False, True)
            residual(BATCHES - 1, 0)
            residual(BATCHES - 1, 1)


def expert_stage(nc, x1, out, comb_dram, gate_w, w_gate, w_up, w_down, sw_gate, sw_up, sw_down, ident_dram):
    x1v = x1.rearrange("(n p) d -> p n d", p=CH)
    outv = out.rearrange("(n p) d -> p n d", p=CH)
    GC = GROUP // CH
    WC = 3 * D
    ctx = ExitStack()
    with ctx:
        def sb(name, shape, dt=F32):
            return ctx.enter_context(nc.sbuf_tensor(name, shape, dt))

        def pb(name, shape):
            return ctx.enter_context(nc.psum_tensor(name, shape, F32))

        def sem(name):
            return ctx.enter_context(nc.semaphore(name))

        ident = sb("f_ident", [128, 128])
        w_raw = [sb(f"f_w_raw{i}", [128, WC]) for i in range(2)]
        w = [sb("f_w_hi", [128, ALL_E, WC], F32R), sb("f_w_lo", [128, ALL_E, WC], F32R)]
        gate_raw = sb("gate_raw", [EXPERTS, D])
        gate_unit = sb("gate_unit", [EXPERTS, D])
        gate_sq = sb("gate_sq", [EXPERTS, D])
        gate_n = sb("gate_n", [EXPERTS, 4])
        gT = [sb("gT_hi", [128, KD, EXPERTS], F32R), sb("gT_lo", [128, KD, EXPERTS], F32R)]
        x_in = sb("f_x_in", [128, GC, D])
        x_res = sb("f_x_res", [128, GC, D])
        x_sq = sb("x_sq", [128, D])
        xT = [[sb(f"f_xT_hi{i}", [128, KD, GROUP], F32R), sb(f"f_xT_lo{i}", [128, KD, GROUP], F32R)] for i in range(2)]
        stats = sb("f_stats", [128, GC, 6])
        mv = sb("f_mv", [128, GC, 2])
        var, rstd, newton = sb("f_var", [128, GC]), sb("f_rstd", [128, GC]), sb("f_newton", [128, GC])
        n2, rnorm, newton_n = sb("n2", [128, GC]), sb("rnorm", [128, GC, 1]), sb("newton_n", [128, GC])
        stats_y = sb("stats_y", [128, GC, 6])
        mv_y = sb("mv_y", [128, GC, 2])
        var_y, rstd_y, newton_y = sb("var_y", [128, GC]), sb("rstd_y", [128, GC]), sb("newton_y", [128, GC])
        logits = sb("logits", [128, GC, EXPERTS])
        scores = sb("scores", [128, GC, EXPERTS])
        top8 = sb("top8", [128, GC, TOPK])
        rest = sb("rest", [128, GC, EXPERTS])
        chosen = sb("chosen", [128, GC, EXPERTS])
        total = sb("total", [128, GC, 1])
        comb = sb("comb", [128, GC, EXPERTS])
        combT = sb("combT", [EXPERTS, GROUP])
        cb = [sb(f"cb{i}", [128, GROUP]) for i in range(4)]
        gate_act = [sb(f"gate_act{i}", [128, GROUP]) for i in range(2)]
        gated = sb("gated", [128, GROUP])
        h32 = [sb(f"h32_{i}", [128, GROUP]) for i in range(2)]
        h = [[sb(f"h_hi{i}", [128, GROUP], F32R), sb(f"h_lo{i}", [128, GROUP], F32R)] for i in range(2)]
        y = sb("y", [128, GC, D])

        g_bank = [pb(f"g_bank{i}", [128, GROUP]) for i in range(2)]
        u_bank = [pb(f"u_bank{i}", [128, GROUP]) for i in range(2)]
        y_bank = pb("y_bank", [128, GC, D])
        job_bank = pb("f_job_bank", [128, 512])

        names = """f_const_loaded w_hi_ready w_split gate_ready gate_chain gate_sq_ready gT_ready gT_hi gT_read
            f_x_loaded f_x_normed ln_chain f_mean_ready xT_ready xT_hi_ready xT_read sq_ready norm_chain
            lg_ready lg_read tanh_ready route_chain cbT_ready cbT_read comb_stored
            gu_ready silu_done gated_done h_done h_hi_done h_ready down_done y_stored y_chain y_mean_ready
            y_normed f_res_loaded out_ready out_stored""".split()
        S = {n: sem(n) for n in names}
        w_loaded = [sem(f"w_loaded{i}") for i in range(2)]
        cb_loaded = [sem(f"cb_loaded{i}") for i in range(4)]
        passed = {e: sem(f"f_passed_{e}") for e in ("dve", "pool", "sp")}

        block = ctx.enter_context(nc.Block())
        INTERLEAVE = 4

        LN = GC + 12
        ROUTE = 1 + 2 * GC + 4

        @block.sync
        def _(sp):
            def load_w(e):
                if e >= 2:
                    sp.wait_ge(S["w_split"], e - 1)
                if e < EXPERTS:
                    parts = (w_gate[e], w_up[e], w_down[e])
                else:
                    parts = (sw_gate, sw_up, sw_down)
                r = w_raw[e % 2]
                sp.dma_start(r[:, 0:D].rearrange("p (k h) -> p k h", k=KD),
                             parts[0].rearrange("(k p) h -> p k h", p=128)).then_inc(w_loaded[e % 2], 16)
                sp.dma_start(r[:, D:2 * D].rearrange("p (k h) -> p k h", k=KD),
                             parts[1].rearrange("(k p) h -> p k h", p=128)).then_inc(w_loaded[e % 2], 16)
                sp.dma_start(r[:, 2 * D:3 * D], parts[2]).then_inc(w_loaded[e % 2], 16)

            def load_x(g):
                sp.dma_start(x_in[:, :, :], x1v[:, bass.ds(g * GC, GC), :]).then_inc(S["f_x_loaded"], 16)

            def store_comb(g):
                wait_apart(sp, S["cbT_read"], g + 1, passed["sp"])
                sp.dma_start(comb_dram[:, bass.ds(g * GROUP, GROUP)], combT[:, :]).then_inc(S["comb_stored"], 16)

            def load_cb(g, e):
                if e == 0:
                    wait_apart(sp, S["comb_stored"], 16 * (g + 1), passed["sp"])
                n = EXPERTS * g + e
                if not (isinstance(n, int) and n < 4):
                    wait_apart(sp, S["h_done"], n - 3, passed["sp"])
                sp.dma_start(cb[e % 4][:, :],
                             comb_dram[e, bass.ds(g * GROUP, GROUP)].partition_broadcast(128)).then_inc(cb_loaded[e % 4], 16)

            def load_res(g):
                wait_apart(sp, S["out_stored"], 16 * (g + 1), passed["sp"])
                sp.dma_start(x_res[:, :, :], x1v[:, bass.ds(g * GC, GC), :]).then_inc(S["f_res_loaded"], 16)

            def store_out(g):
                wait_apart(sp, S["out_ready"], g + 2, passed["sp"])
                sp.dma_start(outv[:, bass.ds(g * GC, GC), :], x_res[:, :, :]).then_inc(S["out_stored"], 16)

            sp.sem_inc(S["out_stored"], 16)
            load_x(0)
            sp.dma_start(ident[:, :], ident_dram).then_inc(S["f_const_loaded"], 16)
            sp.dma_start(gate_raw[:, :], gate_w).then_inc(S["f_const_loaded"], 16)
            for e in range(INTERLEAVE):
                load_w(e)
            sp.wait_ge(S["xT_ready"], KD)
            load_x(1)
            store_comb(0)

            def group(g, first, last):
                for e in range(EXPERTS):
                    load_cb(g, e)
                    if first and e + INTERLEAVE < ALL_E:
                        load_w(e + INTERLEAVE)
                    if e == 1 and not first:
                        load_res(g - 1)
                    if e == 9 and not last:
                        wait_apart(sp, S["xT_ready"], KD * (g + 2), passed["sp"])
                        if isinstance(g, int):
                            if g + 2 < GROUPS:
                                load_x(g + 2)
                        else:
                            load_x(g + 2)
                    if e == 12 and not first:
                        store_out(g - 1)
                if not last:
                    store_comb(g + 1)

            group(0, True, False)
            with sp.Fori(1, GROUPS - 3, 2) as g:
                group(g, False, False)
                group(g + 1, False, False)
            group(GROUPS - 3, False, False)
            group(GROUPS - 2, False, False)
            group(GROUPS - 1, False, True)
            load_res(GROUPS - 1)
            store_out(GROUPS - 1)
            sp.wait_ge(S["out_stored"], 16 * (GROUPS + 1))

        @block.tensor
        def _(pe):
            mm = nc.tensor.matmul
            before = []
            READ = {"XT": "xT_read", "LG": "lg_read", "CB": "cbT_read", "GT": "gT_read"}
            NTH = {"XT": KD, "LG": 1, "CB": 1, "GT": KD}

            def take_bank(kind, g, i):
                if before:
                    k0, g0, i0 = before.pop()
                    pe.wait_ge(S[READ[k0]], NTH[k0] * g0 + i0 + 1)
                before.append((kind, g, i))

            def xt(g, par, k):
                take_bank("XT", g, k)
                pe.wait_ge(S["f_x_normed"], GC * (g + 1))
                for c in range(GC):
                    last = nc.tensor.transpose(job_bank[:, c * CH:(c + 1) * CH], x_in[:, c, k * 128:(k + 1) * 128], ident[:, :])
                last.then_inc(S["xT_ready"], 1)

            def lg(g, par):
                take_bank("LG", g, 0)
                pe.wait_ge(S["xT_read"], KD * (g + 1))
                if isinstance(g, int) and g == 0:
                    pe.wait_ge(S["gT_read"], KD)
                steps = [(k, a, b) for k in range(KD) for a, b in PARTS]
                for c in range(GC):
                    for t, (k, a, b) in enumerate(steps):
                        last = mm(job_bank[:, c * EXPERTS:(c + 1) * EXPERTS], xT[par][a][:, k, c * CH:(c + 1) * CH],
                                  gT[b][:, k, :], start=(t == 0), stop=(t == len(steps) - 1))
                last.then_inc(S["lg_ready"], 1)

            def cbt(g):
                take_bank("CB", g, 0)
                pe.wait_ge(S["route_chain"], ROUTE * (g + 1))
                for c in range(GC):
                    last = nc.tensor.transpose(job_bank[0:EXPERTS, c * CH:(c + 1) * CH], comb[:, c, :], ident[:, :])
                last.then_inc(S["cbT_ready"], 1)

            def gu(g, par, e, first):
                n = ALL_E * g + e
                if first:
                    pe.wait_ge(S["w_split"], e + 1)
                if e == 0:
                    pe.wait_ge(S["xT_read"], KD * (g + 1))
                if not (isinstance(n, int) and n < 2):
                    pe.wait_ge(S["gated_done"], n - 1)
                i = (e + par) % 2
                steps = [(k, a, b) for k in range(KD) for a, b in PARTS]
                for bank, col in ((g_bank[i], 0), (u_bank[i], D)):
                    for t, (k, a, b) in enumerate(steps):
                        last = mm(bank[:, :], w[b][:, e, col + k * HID:col + (k + 1) * HID], xT[par][a][:, k, :],
                                  start=(t == 0), stop=(t == len(steps) - 1))
                last.then_inc(S["gu_ready"], 1)

            def down(g, par, e):
                n = ALL_E * g + e
                pe.wait_ge(S["h_ready"], n + 1)
                if e == 0 and not (isinstance(g, int) and g == 0):
                    pe.wait_ge(S["y_stored"], 2 * g)
                i = (e + par) % 2
                for c in range(GC):
                    for t, (a, b) in enumerate(PARTS):
                        last = mm(y_bank[:, c, :], h[i][a][:, c * CH:(c + 1) * CH], w[b][:, e, 2 * D:3 * D],
                                  start=(e == 0 and t == 0 and c % 2 == 0), stop=(e == ALL_E - 1 and t == 2),
                                  skip_group_check=True)
                last.then_inc(S["down_done"], 1)

            pe.wait_ge(S["f_const_loaded"], 32)
            for k in range(KD):
                take_bank("GT", 0, k)
                pe.wait_ge(S["gate_ready"], 1)
                nc.tensor.transpose(job_bank[:, 0:EXPERTS], gate_unit[:, k * 128:(k + 1) * 128],
                                    ident[0:EXPERTS, 0:EXPERTS]).then_inc(S["gT_ready"], 1)
            for k in range(KD):
                xt(0, 0, k)
            lg(0, 0)
            gu(0, 0, 0, True)
            gu(0, 0, 1, True)
            cbt(0)

            def group(g, par, first, last):
                if not first:
                    before.clear()
                    before.append(("CB", g, 0))
                for e in range(ALL_E):
                    if e + 2 < ALL_E:
                        gu(g, par, e + 2, first)
                    elif not last:
                        gu(g + 1, 1 - par, e + 2 - ALL_E, False)
                    if not last and e in (4, 6):
                        xt(g + 1, 1 - par, (e - 4) // 2)
                    if not last and e == 8:
                        lg(g + 1, 1 - par)
                    down(g, par, e)
                    if not last and e == 13:
                        cbt(g + 1)

            group(0, 0, True, False)
            with pe.Fori(1, GROUPS - 3, 2) as g:
                group(g, 1, False, False)
                group(g + 1, 0, False, False)
            group(GROUPS - 3, 1, False, False)
            group(GROUPS - 2, 0, False, False)
            group(GROUPS - 1, 1, False, True)

        @block.scalar
        def _(act):
            a_ = nc.scalar.activation

            def split_hi(e):
                act.wait_ge(w_loaded[e % 2], 48 * (e // 2 + 1))
                a_(w[0][:, e, :], w_raw[e % 2][:, :], ACT.Copy).then_inc(S["w_hi_ready"], 1)

            def xt_hi(g, par, k):
                act.wait_ge(S["xT_ready"], KD * g + k + 1)
                if not (isinstance(g, int) and g < 2):
                    act.wait_ge(S["gu_ready"], ALL_E * (g - 1))
                a_(xT[par][0][:, k, :], job_bank[:, :], ACT.Identity).then_inc(S["xT_hi_ready"], 1)

            def squares(g, c):
                act.wait_ge(S["f_x_normed"], GC * (g + 1))
                if c == 0 and not (isinstance(g, int) and g == 0):
                    act.wait_ge(S["norm_chain"], 12 * g)
                n = GC * g + c
                if not (isinstance(n, int) and n == 0):
                    act.wait_ge(S["sq_ready"], n)
                a_(x_sq[:, :], x_in[:, c, :], ACT.Square, accum_out=n2[:, c:c + 1]).then_inc(S["sq_ready"], 1)

            def tanh(g):
                act.wait_ge(S["lg_read"], g + 1)
                if not (isinstance(g, int) and g == 0):
                    act.wait_ge(S["route_chain"], ROUTE * g)
                a_(scores[:, :, :], logits[:, :, :], ACT.Tanh, scale=0.5).then_inc(S["tanh_ready"], 1)

            def silu(g, par, e):
                n = ALL_E * g + e
                act.wait_ge(S["gu_ready"], n + 1)
                if not (isinstance(n, int) and n < 2):
                    act.wait_ge(S["gated_done"], n - 1)
                i = (e + par) % 2
                a_(gate_act[i][:, :], g_bank[i][:, :], ACT.Silu).then_inc(S["silu_done"], 1)

            def h_hi(g, par, e):
                n = ALL_E * g + e
                if e < EXPERTS:
                    act.wait_ge(S["h_done"], EXPERTS * g + e + 1)
                else:
                    act.wait_ge(S["gated_done"], n + 1)
                if not (isinstance(n, int) and n < 2):
                    act.wait_ge(S["down_done"], n - 1)
                i = (e + par) % 2
                a_(h[i][0][:, :], h32[i][:, :], ACT.Copy).then_inc(S["h_hi_done"], 1)

            def store_y(g):
                act.wait_ge(S["down_done"], ALL_E * (g + 1))
                act.wait_ge(S["out_ready"], g + 1)
                for i in range(2):
                    a_(y[:, 2 * i:2 * i + 2, :], y_bank[:, 2 * i:2 * i + 2, :], ACT.Copy).then_inc(S["y_stored"], 1)

            act.wait_ge(S["f_const_loaded"], 32)
            a_(gate_sq[:, :], gate_raw[:, :], ACT.Square, accum_out=gate_n[:, 0:1]).then_inc(S["gate_sq_ready"], 1)
            for c in range(GC):
                squares(0, c)
            for k in range(KD):
                act.wait_ge(S["gT_ready"], k + 1)
                a_(gT[0][:, k, :], job_bank[:, 0:EXPERTS], ACT.Identity).then_inc(S["gT_hi"], 1)
            for k in range(KD):
                xt_hi(0, 0, k)
            for e in range(INTERLEAVE):
                split_hi(e)
            tanh(0)

            def group(g, par, first, last):
                for e in range(ALL_E):
                    silu(g, par, e)
                    if e > 0:
                        h_hi(g, par, e - 1)
                    elif not first:
                        h_hi(g - 1, 1 - par, ALL_E - 1)
                    if e == 1 and not first:
                        store_y(g - 1)
                    if first and e + INTERLEAVE < ALL_E:
                        split_hi(e + INTERLEAVE)
                    if not last:
                        if e in (5, 6):
                            squares(g + 1, 2 * (e - 5))
                            squares(g + 1, 2 * (e - 5) + 1)
                        if e in (7, 9):
                            xt_hi(g + 1, 1 - par, (e - 7) // 2)
                        if e == 12:
                            tanh(g + 1)

            group(0, 0, True, False)
            with act.Fori(1, GROUPS - 3, 2) as g:
                group(g, 1, False, False)
                group(g + 1, 0, False, False)
            group(GROUPS - 3, 1, False, False)
            group(GROUPS - 2, 0, False, False)
            group(GROUPS - 1, 1, False, True)
            h_hi(GROUPS - 1, 1, ALL_E - 1)
            store_y(GROUPS - 1)

        @block.vector
        def _(dve):
            v = nc.vector

            def split_lo(e):
                dve.wait_ge(S["w_hi_ready"], e + 1)
                v.tensor_tensor(w[1][:, e, :], w_raw[e % 2][:, :], w[0][:, e, :].bitcast(F32),
                                ALU.subtract).then_inc(S["w_split"], 1)

            def rsqrt_step(n, dst, var_, source, guard, tmp, chain, base):
                if not (isinstance(base, int) and base + n == 0):
                    dve.wait_ge(chain, base + n)
                if n == 0:
                    ins = v.tensor_scalar(var_, source, guard[0], None, guard[1])
                elif n == 1:
                    ins = v.tensor_scalar(dst.bitcast(I32), var_.bitcast(I32), 1, None, ALU.logical_shift_right)
                elif n == 2:
                    ins = v.tensor_scalar(dst.bitcast(I32), dst.bitcast(I32), -1, RSQRT_SEED, ALU.mult, ALU.add)
                elif n % 3 == 0:
                    ins = v.scalar_tensor_tensor(tmp, dst, -0.5, dst, ALU.mult, ALU.mult)
                elif n % 3 == 1:
                    ins = v.tensor_tensor(tmp, tmp, var_, ALU.mult)
                else:
                    ins = v.scalar_tensor_tensor(dst, tmp, 1.5, dst, ALU.add, ALU.mult)
                ins.then_inc(chain, 1)

            def ln_stats(g, first_group):
                dve.wait_ge(S["f_x_loaded"], 16 * (g + 1))
                if not first_group:
                    dve.wait_ge(S["f_x_normed"], GC * g)
                for c in range(GC):
                    v.bn_stats(stats[:, c, :], x_in[:, c, :]).then_inc(S["ln_chain"], 1)
                for c in range(GC):
                    wait_apart(dve, S["ln_chain"], LN * g + c + 1, passed["dve"])
                    v.bn_aggr(mv[:, c, :], stats[:, c, :]).then_inc(S["f_mean_ready"], 1)

            def ln_rstd(g, n):
                if n == 0:
                    dve.wait_ge(S["f_mean_ready"], GC * (g + 1))
                rsqrt_step(n, rstd[:, :], var[:, :], mv[:, :, 1], (EPS, ALU.add), newton[:, :],
                           S["ln_chain"], LN * g + GC)

            def norm_step(g, n):
                if n == 0:
                    dve.wait_ge(S["sq_ready"], GC * (g + 1))
                    if not (isinstance(g, int) and g == 0):
                        dve.wait_ge(S["lg_read"], g)
                rsqrt_step(n, rnorm[:, :, 0], n2[:, :], n2[:, :], (1e-24, ALU.max), newton_n[:, :],
                           S["norm_chain"], 12 * g)

            def xt_lo(g, par, k):
                dve.wait_ge(S["xT_hi_ready"], KD * g + k + 1)
                v.tensor_tensor(xT[par][1][:, k, :], job_bank[:, :], xT[par][0][:, k, :].bitcast(F32),
                                ALU.subtract).then_inc(S["xT_read"], 1)

            def scale_logits(g):
                dve.wait_ge(S["lg_ready"], g + 1)
                dve.wait_ge(S["norm_chain"], 12 * (g + 1))
                if not (isinstance(g, int) and g == 0):
                    dve.wait_ge(S["tanh_ready"], g)
                v.tensor_tensor(logits[:, :, :], job_bank[:, 0:GC * EXPERTS].rearrange("p (c e) -> p c e", c=GC),
                                rnorm[:, :, :].to_broadcast([128, GC, EXPERTS]), ALU.mult).then_inc(S["lg_read"], 1)

            def route_step(g, n):
                chain, base = S["route_chain"], ROUTE * g
                if n == 0:
                    dve.wait_ge(S["tanh_ready"], g + 1)
                if n:
                    wait_apart(dve, chain, base + n, passed["dve"])
                if n == 0:
                    ins = v.tensor_scalar(scores[:, :, :], scores[:, :, :], 0.5, 0.5, ALU.mult, ALU.add)
                elif n <= 4:
                    ins = v.max(out=top8[:, n - 1, :], in_=scores[:, n - 1, :])
                elif n <= 8:
                    ins = v.match_replace(out=rest[:, n - 5, :], in_to_replace=top8[:, n - 5, :],
                                          in_values=scores[:, n - 5, :], imm_value=0.0)
                elif n == 9:
                    ins = v.tensor_tensor(chosen[:, :, :], scores[:, :, :], rest[:, :, :], ALU.subtract)
                elif n == 10:
                    ins = v.reduce_sum(total[:, :, 0], chosen[:, :, :], AX_X)
                elif n == 11:
                    ins = v.reciprocal(total[:, :, :], total[:, :, :])
                elif n == 12:
                    if not (isinstance(g, int) and g == 0):
                        dve.wait_ge(S["cbT_ready"], g)
                    ins = v.tensor_tensor(comb[:, :, :], chosen[:, :, :],
                                          total[:, :, :].to_broadcast([128, GC, EXPERTS]), ALU.mult)
                ins.then_inc(chain, 1)

            def cbt_copy(g):
                dve.wait_ge(S["cbT_ready"], g + 1)
                if not (isinstance(g, int) and g == 0):
                    dve.wait_ge(S["comb_stored"], 16 * g)
                v.tensor_copy(combT[:, :], job_bank[0:EXPERTS, :]).then_inc(S["cbT_read"], 1)

            def gate(g, par, e):
                n = ALL_E * g + e
                i = (e + par) % 2
                dve.wait_ge(S["silu_done"], n + 1)
                if not (isinstance(n, int) and n < 2):
                    dve.wait_ge(S["h_ready"], n - 1)
                if e < EXPERTS:
                    if not (isinstance(n, int) and n == 0):
                        dve.wait_ge(S["h_done"], EXPERTS * g + e)
                    v.tensor_tensor(gated[:, :], gate_act[i][:, :], u_bank[i][:, :], ALU.mult).then_inc(S["gated_done"], 1)
                    dve.wait_ge(S["gated_done"], n + 1)
                    dve.wait_ge(cb_loaded[e % 4], 16 * (EXPERTS // 4 * g + e // 4 + 1))
                    v.tensor_tensor(h32[i][:, :], gated[:, :], cb[e % 4][:, :], ALU.mult).then_inc(S["h_done"], 1)
                else:
                    v.tensor_tensor(h32[i][:, :], gate_act[i][:, :], u_bank[i][:, :], ALU.mult).then_inc(S["gated_done"], 1)

            def h_lo(g, par, e):
                n = ALL_E * g + e
                i = (e + par) % 2
                dve.wait_ge(S["h_hi_done"], n + 1)
                v.tensor_tensor(h[i][1][:, :], h32[i][:, :], h[i][0][:, :].bitcast(F32),
                                ALU.subtract).then_inc(S["h_ready"], 1)

            def y_stats(g):
                dve.wait_ge(S["y_stored"], 2 * (g + 1))
                for c in range(GC):
                    v.bn_stats(stats_y[:, c, :], y[:, c, :]).then_inc(S["y_chain"], 1)
                for c in range(GC):
                    wait_apart(dve, S["y_chain"], LN * g + c + 1, passed["dve"])
                    v.bn_aggr(mv_y[:, c, :], stats_y[:, c, :]).then_inc(S["y_mean_ready"], 1)

            def y_rstd(g, n):
                if n == 0:
                    dve.wait_ge(S["y_mean_ready"], GC * (g + 1))
                rsqrt_step(n, rstd_y[:, :], var_y[:, :], mv_y[:, :, 1], (EPS, ALU.add), newton_y[:, :],
                           S["y_chain"], LN * g + GC)

            ln_stats(0, True)
            for n in range(12):
                ln_rstd(0, n)
            dve.wait_ge(S["gate_sq_ready"], 1)
            for n in range(12):
                rsqrt_step(n, gate_n[:, 1:2], gate_n[:, 0:1], gate_n[:, 0:1], (1e-24, ALU.max), gate_n[:, 2:3],
                           S["gate_chain"], 0)
            dve.wait_ge(S["gate_chain"], 12)
            v.tensor_scalar(gate_unit[:, :], gate_raw[:, :], gate_n[:, 1:2], None, ALU.mult).then_inc(S["gate_ready"], 1)
            for k in range(KD):
                dve.wait_ge(S["gT_hi"], k + 1)
                v.tensor_tensor(gT[1][:, k, :], job_bank[:, 0:EXPERTS], gT[0][:, k, :].bitcast(F32),
                                ALU.subtract).then_inc(S["gT_read"], 1)
            for n in range(12):
                norm_step(0, n)
            for k in range(KD):
                xt_lo(0, 0, k)
            for e in range(INTERLEAVE):
                split_lo(e)
            scale_logits(0)
            for n in range(ROUTE):
                route_step(0, n)
            cbt_copy(0)

            def group(g, par, first, last):
                for e in range(ALL_E):
                    gate(g, par, e)
                    if e > 0:
                        h_lo(g, par, e - 1)
                    elif not first:
                        h_lo(g - 1, 1 - par, ALL_E - 1)
                    if first and e + INTERLEAVE < ALL_E:
                        split_lo(e + INTERLEAVE)
                    if not last:
                        if e == 0:
                            ln_stats(g + 1, False)
                        if e in (1, 2, 3):
                            for n in range(4):
                                ln_rstd(g + 1, 4 * (e - 1) + n)
                        if e in (7, 9):
                            xt_lo(g + 1, 1 - par, (e - 7) // 2)
                        if e in (7, 8):
                            for n in range(6):
                                norm_step(g + 1, 6 * (e - 7) + n)
                        if e == 11:
                            scale_logits(g + 1)
                        if e in (12, 13, 14):
                            for n in range(5 * (e - 12), min(5 * (e - 11), ROUTE)):
                                route_step(g + 1, n)
                        if e == 16:
                            cbt_copy(g + 1)
                    if not first:
                        if e == 4:
                            y_stats(g - 1)
                        if e in (4, 5, 6):
                            for n in range(4):
                                y_rstd(g - 1, 4 * (e - 4) + n)

            group(0, 0, True, False)
            with dve.Fori(1, GROUPS - 3, 2) as g:
                group(g, 1, False, False)
                group(g + 1, 0, False, False)
            group(GROUPS - 3, 1, False, False)
            group(GROUPS - 2, 0, False, False)
            group(GROUPS - 1, 1, False, True)
            h_lo(GROUPS - 1, 1, ALL_E - 1)
            y_stats(GROUPS - 1)
            for n in range(12):
                y_rstd(GROUPS - 1, n)

        @block.gpsimd
        def _(pool):
            gp = nc.gpsimd

            def norm_x(g):
                wait_apart(pool, S["ln_chain"], LN * (g + 1), passed["pool"])
                for c in range(GC):
                    gp.tensor_scalar(x_in[:, c, :], x_in[:, c, :], mv[:, c, 0:1], rstd[:, c:c + 1],
                                     ALU.subtract, ALU.mult).then_inc(S["f_x_normed"], 1)

            def finish(g):
                wait_apart(pool, S["y_chain"], LN * (g + 1), passed["pool"])
                for c in range(GC):
                    gp.tensor_scalar(y[:, c, :], y[:, c, :], mv_y[:, c, 0:1], rstd_y[:, c:c + 1],
                                     ALU.subtract, ALU.mult).then_inc(S["y_normed"], 1)
                wait_apart(pool, S["f_res_loaded"], 16 * (g + 1), passed["pool"])
                wait_apart(pool, S["y_normed"], GC * (g + 1), passed["pool"])
                gp.tensor_tensor(x_res[:, :, :], y[:, :, :], x_res[:, :, :], ALU.add).then_inc(S["out_ready"], 1)

            pool.sem_inc(S["out_ready"], 1)
            norm_x(0)

            def group(g, first, last):
                if not last:
                    norm_x(g + 1)
                if not first:
                    finish(g - 1)

            group(0, True, False)
            with pool.Fori(1, GROUPS - 1) as g:
                group(g, False, False)
            group(GROUPS - 1, False, True)
            finish(GROUPS - 1)


def kernel(**inputs):
    import numpy as np
    import concourse.bacc as bacc
    from concourse.bass_utils import run_bass_kernel_spmd

    nc = bacc.Bacc("TRN2", target_bir_lowering=False, num_devices=1)
    a = {n: np.asarray(v) for n, v in inputs.items() if n != "L0_attn_mask"}
    laid = {
        "x": a["L0_attn_query"].reshape(TOKENS, D),
        "wq": a["L0_attn_q_w"].T, "wk": a["L0_attn_k_w"].T, "wv": a["L0_attn_v_w"].T, "wo": a["L0_attn_out_w"].T,
        "biases": np.stack([a[f"L0_attn_{n}_b"] for n in "qkv"]).reshape(3, KD, 128).transpose(2, 0, 1),
        "ob": a["L0_attn_out_b"],
        "gate_w": a["L0_ffn_gate_w"], "w_gate": a["L0_ffn_w_gate"], "w_up": a["L0_ffn_w_up"], "w_down": a["L0_ffn_w_down"],
        "sw_gate": a["L0_ffn_sw_gate"], "sw_up": a["L0_ffn_sw_up"], "sw_down": a["L0_ffn_sw_down"],
        "ident": np.eye(128, dtype=np.float32),
    }
    laid = {n: np.ascontiguousarray(v) for n, v in laid.items()}
    t = {n: nc.dram_tensor(f"in_{n}", v.shape, mybir.dt.from_np(v.dtype), kind="ExternalInput").ap() for n, v in laid.items()}
    out = nc.dram_tensor("out", (TOKENS, D), F32, kind="ExternalOutput").ap()
    x1 = nc.dram_tensor("x1", (TOKENS, D), F32).ap()
    comb_dram = nc.dram_tensor("comb_dram", (EXPERTS, TOKENS), F32).ap()
    attention_stage(nc, t["x"], x1, t["wq"], t["wk"], t["wv"], t["wo"], t["biases"], t["ob"], t["ident"])
    expert_stage(nc, x1, out, comb_dram, t["gate_w"], t["w_gate"], t["w_up"], t["w_down"],
                 t["sw_gate"], t["sw_up"], t["sw_down"], t["ident"])
    r = run_bass_kernel_spmd(nc, [{f"in_{n}": v for n, v in laid.items()}], core_ids=[0])
    return r.results[0]["out"].reshape(BATCHES, SEQ, D)
```
